# Optimizing a Trainium2 kernel written in Bass

```python
import numpy as np
import jax
import jax.numpy as jnp

def _softmax(x, axis=-1):
    return jax.nn.softmax(x, axis=axis)

def _gelu(x):
    return jax.nn.gelu(x, approximate=True)

def _silu(x):
    return jax.nn.silu(x)

def _sigmoid(x):
    return jax.nn.sigmoid(x)

def _layernorm(x, axis=-1, eps=1e-05):
    m = jnp.mean(x, axis=axis, keepdims=True)
    v = jnp.var(x, axis=axis, keepdims=True)
    return (x - m) / jnp.sqrt(v + eps)

def _scatter_add(tgt, idx, src, axis=0):
    return tgt.at[idx].add(src)

def _segment_sum(src, seg, n):
    return jax.ops.segment_sum(src, seg, n)
kernel_name = 'mk_seq_preln_d1_jaxref_r8_404764'

def setup_inputs(seed: int=0):
    np.random.seed(seed)
    _w = jnp.asarray

    def _L0_attn_setup():
        import jax, jax.numpy as jnp
        import numpy as np
        NUM_HEADS = 8
        CHUNK = 64

        def _retention(q, k, v):
            B, Hn, L, DK = q.shape
            DV = v.shape[-1]
            C = CHUNK
            N = L // C
            dt = q.dtype
            gamma = (1.0 - jnp.exp2(-5.0 - jnp.arange(Hn, dtype=jnp.float32))).astype(dt)
            q = q * DK ** (-0.5)
            idx = jnp.arange(C)
            diff = idx[:, None] - idx[None, :]
            D = jnp.where(diff >= 0, gamma[:, None, None] ** diff, 0.0).astype(dt)
            decay_q = (gamma[:, None] ** (idx[None, :] + 1)).astype(dt)
            decay_k = (gamma[:, None] ** (C - 1 - idx[None, :])).astype(dt)
            decay_s = (gamma ** C).astype(dt)

            def to_chunks(x):
                return jnp.moveaxis(x.reshape(B, Hn, N, C, -1), 2, 0)
            qs, ks, vs = map(to_chunks, (q, k, v))

            def step(S, x):
                qc, kc, vc = x
                attn = jnp.einsum('bhid,bhjd->bhij', qc, kc) * D
                o_intra = jnp.einsum('bhij,bhje->bhie', attn, vc)
                o_inter = jnp.einsum('bhid,bhde->bhie', qc * decay_q[None, :, :, None], S)
                S_new = decay_s[None, :, None, None] * S + jnp.einsum('bhjd,bhje->bhde', kc * decay_k[None, :, :, None], vc)
                return (S_new, o_intra + o_inter)
            S0 = jnp.zeros((B, Hn, DK, DV), dt)
            _, o = jax.lax.scan(step, S0, (qs, ks, vs))
            return jnp.moveaxis(o, 0, 2).reshape(B, Hn, L, DV)

        def _xavier(key, fan_in, fan_out, gain=2 ** (-2.5)):
            limit = gain * np.sqrt(6.0 / (fan_in + fan_out))
            return jax.random.uniform(key, (fan_in, fan_out), jnp.float32, -limit, limit)
        key = jax.random.key(seed)
        k0, k1, k2, k3, k4 = jax.random.split(key, 5)
        B, L, D = (2, 512, 128)
        return {'hidden_states': jax.random.normal(k0, (B, L, D), jnp.float32), 'rel_pos': jnp.zeros((1,), jnp.float32), 'Wq': _xavier(k1, D, D), 'Wk': _xavier(k2, D, D), 'Wv': _xavier(k3, D, D), 'Wo': _xavier(k4, D, D)}
    _L0_attn_in = _L0_attn_setup()

    def _L0_ffn_setup():
        import jax, jax.numpy as jnp
        import numpy as np
        TOP_K = 2
        key = jax.random.key(seed)
        kx, kg, k1, k2 = jax.random.split(key, 4)
        B, T, D, E, H = (4, 128, 128, 8, 256)
        x = jax.random.normal(kx, (B, T, D), dtype=jnp.float32)
        Wg = jax.random.normal(kg, (D, E), dtype=jnp.float32) * 0.02
        W1 = jax.random.normal(k1, (E, D, H), dtype=jnp.float32) * 0.02
        W2 = jax.random.normal(k2, (E, H, D), dtype=jnp.float32) * 0.02
        return {'x': x, 'Wg': Wg, 'W1': W1, 'W2': W2}
    _L0_ffn_in = _L0_ffn_setup()
    _d = {'L0_attn_hidden_states': _L0_attn_in['hidden_states'], 'L0_attn_rel_pos': _L0_attn_in['rel_pos'], 'L0_attn_Wq': _L0_attn_in['Wq'], 'L0_attn_Wk': _L0_attn_in['Wk'], 'L0_attn_Wv': _L0_attn_in['Wv'], 'L0_attn_Wo': _L0_attn_in['Wo'], 'L0_ffn_Wg': _L0_ffn_in['Wg'], 'L0_ffn_W1': _L0_ffn_in['W1'], 'L0_ffn_W2': _L0_ffn_in['W2']}
    _x0 = _d['L0_attn_hidden_states']
    _d['L0_attn_hidden_states'] = jax.random.normal(jax.random.fold_in(jax.random.key(seed), 1), (2, 2048, 128), dtype=_x0.dtype)
    del _x0
    return _d

def reference(L0_attn_hidden_states, L0_attn_rel_pos, L0_attn_Wq, L0_attn_Wk, L0_attn_Wv, L0_attn_Wo, L0_ffn_Wg, L0_ffn_W1, L0_ffn_W2):

    def _L0_attn_ref(hidden_states, rel_pos, Wq, Wk, Wv, Wo):
        import jax, jax.numpy as jnp
        import numpy as np
        NUM_HEADS = 8
        CHUNK = 64

        def _retention(q, k, v):
            B, Hn, L, DK = q.shape
            DV = v.shape[-1]
            C = CHUNK
            N = L // C
            dt = q.dtype
            gamma = (1.0 - jnp.exp2(-5.0 - jnp.arange(Hn, dtype=jnp.float32))).astype(dt)
            q = q * DK ** (-0.5)
            idx = jnp.arange(C)
            diff = idx[:, None] - idx[None, :]
            D = jnp.where(diff >= 0, gamma[:, None, None] ** diff, 0.0).astype(dt)
            decay_q = (gamma[:, None] ** (idx[None, :] + 1)).astype(dt)
            decay_k = (gamma[:, None] ** (C - 1 - idx[None, :])).astype(dt)
            decay_s = (gamma ** C).astype(dt)

            def to_chunks(x):
                return jnp.moveaxis(x.reshape(B, Hn, N, C, -1), 2, 0)
            qs, ks, vs = map(to_chunks, (q, k, v))

            def step(S, x):
                qc, kc, vc = x
                attn = jnp.einsum('bhid,bhjd->bhij', qc, kc) * D
                o_intra = jnp.einsum('bhij,bhje->bhie', attn, vc)
                o_inter = jnp.einsum('bhid,bhde->bhie', qc * decay_q[None, :, :, None], S)
                S_new = decay_s[None, :, None, None] * S + jnp.einsum('bhjd,bhje->bhde', kc * decay_k[None, :, :, None], vc)
                return (S_new, o_intra + o_inter)
            S0 = jnp.zeros((B, Hn, DK, DV), dt)
            _, o = jax.lax.scan(step, S0, (qs, ks, vs))
            return jnp.moveaxis(o, 0, 2).reshape(B, Hn, L, DV)

        def _xavier(key, fan_in, fan_out, gain=2 ** (-2.5)):
            limit = gain * np.sqrt(6.0 / (fan_in + fan_out))
            return jax.random.uniform(key, (fan_in, fan_out), jnp.float32, -limit, limit)
        B, L, Dm = hidden_states.shape
        Hd = Dm // NUM_HEADS
        q = (hidden_states @ Wq).reshape(B, L, NUM_HEADS, Hd).transpose(0, 2, 1, 3)
        k = (hidden_states @ Wk).reshape(B, L, NUM_HEADS, Hd).transpose(0, 2, 1, 3)
        v = (hidden_states @ Wv).reshape(B, L, NUM_HEADS, Hd).transpose(0, 2, 1, 3)
        o = _retention(q, k, v)
        o = o.transpose(0, 2, 1, 3).reshape(B, L, Dm)
        return o @ Wo

    def _L0_ffn_ref(x, Wg, W1, W2):
        import jax, jax.numpy as jnp
        import numpy as np
        TOP_K = 2
        B, T, D = x.shape
        E = W1.shape[0]
        logits = jnp.einsum('btd,de->bte', x, Wg)
        probs = jax.nn.softmax(logits, axis=-1)
        top_w, top_i = jax.lax.top_k(probs, TOP_K)
        top_w = top_w / (jnp.sum(top_w, axis=-1, keepdims=True) + 1e-08)
        N = B * T
        oh = jax.nn.one_hot(top_i.reshape(N, TOP_K), E, dtype=x.dtype)
        combine = jnp.sum(oh * top_w.reshape(N, TOP_K)[..., None], axis=1)
        xt = x.reshape(N, D)
        h = jnp.einsum('td,edh->teh', xt, W1)
        h = jnp.square(jax.nn.relu(h))
        y = jnp.einsum('teh,ehd->ted', h, W2)
        out = jnp.einsum('te,ted->td', combine, y)
        return out.reshape(B, T, D)
    x = L0_attn_hidden_states
    x = x + _L0_attn_ref(_layernorm(x, axis=-1), L0_attn_rel_pos, L0_attn_Wq, L0_attn_Wk, L0_attn_Wv, L0_attn_Wo)
    x = x + _L0_ffn_ref(_layernorm(x, axis=-1), L0_ffn_Wg, L0_ffn_W1, L0_ffn_W2)
    return x

_drawn_inputs = setup_inputs


def setup_inputs(seed=0):
    import zlib

    import numpy as np

    out = dict(_drawn_inputs(seed))
    spreads = {}
    factors = {'L0_ffn_Wg': 4.553, 'L0_ffn_W1': 4.373, 'L0_ffn_W2': 4.04}
    for name, (base, spread) in spreads.items():
        noise = np.random.default_rng([zlib.crc32(name.encode()), seed]).standard_normal(out[name].shape)
        drawn = base * np.exp(spread * noise) if base else spread * noise
        out[name] = jnp.asarray(drawn.astype(out[name].dtype))
    for name, factor in factors.items():
        out[name] = (out[name] * factor).astype(out[name].dtype)
    return out
```

```python
from contextlib import ExitStack

import concourse.bass as bass
from concourse import mybir

F32 = mybir.dt.float32
F32R = mybir.dt.float32r
U32 = mybir.dt.uint32
ALU = mybir.AluOpType
ACT = mybir.ActivationFunctionType
AX_X = mybir.AxisListType.X

P = 128
HEADS = 8
DH = P // HEADS
CHUNK = 64
PAIRS = HEADS // 2
PW = 2 * DH
TILE = 512
GROUPS = TILE // P
CHUNKS = TILE // CHUNK
EXPERTS = 8
HIDDEN = 256
HALVES = HIDDEN // P
LN_EPS = 1e-5
TOP_EPS = 1e-8
BIG = 3.4028234e38
DMA = 16

C_IDENT = 0
C_DECAY = C_IDENT + P
C_DQ = C_DECAY + HEADS * CHUNK
C_DK = C_DQ + CHUNK
C_EVEN = C_DK + P
C_ODD = C_EVEN + 1
C_DS = C_ODD + 1
C_SMASK = C_DS + 1
C_LOW = C_SMASK + PW
C_HIGH = C_LOW + 8
C_IOTA = C_HIGH + 8
C_MHALF = C_IOTA + EXPERTS
C_HALF = C_MHALF + GROUPS
C_ALL = C_HALF + GROUPS * EXPERTS


class Tile:

    def __init__(self, pair, k, first):
        self.pair, self.k, self.first = pair, k, first
        self.index = pair * 2 + k
        self.parity = k % 2
        self.exists = first >= 0

    def back(self, n):
        return Tile(self.pair, self.k - n, self.first - n)

    def count(self, per_tile, n=None):
        return self.pair * (2 * per_tile) + (self.k * per_tile + (per_tile if n is None else n))

    def count2(self, per_tile):
        return self.pair * per_tile + (self.k // 2 + 1) * per_tile


def tile(n):
    return Tile(n // 2, n % 2, n)


NONE = Tile(0, -9, -9)


def build(nc, x, wq, wk, wv, wo, wg, w1, w2, constants, scratch, out):
    tokens = x.shape[0] * x.shape[1]
    tiles = tokens // TILE
    assert tiles == 8 and x.shape[2] == P
    x_t = x.rearrange("b (t g p) d -> (b t) p g d", g=GROUPS, p=P)
    out_t = out.rearrange("b (t g p) d -> (b t) p g d", g=GROUPS, p=P)
    row = EXPERTS * TILE

    with ExitStack() as ctx:
        def sb(name, shape, dt=F32):
            return ctx.enter_context(nc.sbuf_tensor(name, shape, dt))

        def sem(name):
            return ctx.enter_context(nc.semaphore(name))

        cst = sb("cst", [P, C_ALL])
        w_attn = sb("w_attn", [P, 4, P])
        wg_in = sb("wg_in", [P, EXPERTS])
        wg_hi, wg_lo = (sb(n, [P, EXPERTS], F32R) for n in ("wg_hi", "wg_lo"))
        w1_in = sb("w1_in", [P, EXPERTS, HIDDEN])
        w1_hi, w1_lo = (sb(n, [P, EXPERTS, HIDDEN], F32R) for n in ("w1_hi", "w1_lo"))
        w2_in = sb("w2_in", [P, EXPERTS * HALVES, P])
        w2_hi, w2_lo = (sb(n, [P, EXPERTS * HALVES, P], F32R) for n in ("w2_hi", "w2_lo"))

        x_in = sb("x_in", [P, 2, GROUPS, P])
        stats = sb("stats", [P, 2, GROUPS, 6])
        moments = sb("moments", [P, 2, GROUPS, 2])
        variance = sb("variance", [P, 2, GROUPS])
        rstd = sb("rstd", [P, 2, GROUPS])
        xn1 = sb("xn1", [P, GROUPS, P])
        xn1_t = sb("xn1_t", [P, TILE])
        q_m = sb("q_m", [P, 2, TILE])
        q_d = sb("q_d", [P, TILE])
        k_t = sb("k_t", [P, TILE])
        k_d = sb("k_d", [P, GROUPS, P])
        v_z = sb("v_z", [P, GROUPS * PAIRS, 4, DH])
        attn = sb("attn", [P, PAIRS, GROUPS, 2, CHUNK])
        state = sb("state", [P, CHUNKS + 1, PW])
        state_m = sb("state_m", [P, CHUNKS, PW])
        o_t = sb("o_t", [P, GROUPS, 2, CHUNK])
        x2 = sb("x2", [P, 2, GROUPS, P])
        xn2 = sb("xn2", [P, GROUPS, P])
        x_hi = sb("x_hi", [P, 2, TILE], F32R)
        x_lo = sb("x_lo", [P, 2, TILE], F32R)
        top = sb("top", [P, GROUPS])
        logits = sb("logits", [P, GROUPS, EXPERTS])
        expd = sb("expd", [P, GROUPS, EXPERTS])
        total = sb("total", [P, GROUPS])
        best = sb("best", [P, GROUPS, 8])
        best_at = sb("best_at", [P, GROUPS, 8], U32)
        best_f = sb("best_f", [P, GROUPS, 2])
        denom = sb("denom", [P, 2, GROUPS])
        r_denom = sb("r_denom", [P, GROUPS])
        chosen = sb("chosen", [P, 3, GROUPS, EXPERTS])
        share = sb("share", [P, GROUPS, EXPERTS])
        combine = sb("combine", [P, EXPERTS, GROUPS])
        combine_r = sb("combine_r", [P, EXPERTS, GROUPS])
        combine_t = sb("combine_t", [EXPERTS * GROUPS, P])
        scale = sb("scale", [P, 2, EXPERTS, TILE])
        act_s = sb("act_s", [P, 2, HALVES, TILE])
        act_f = sb("act_f", [P, 2, HALVES, TILE])
        act_hi = sb("act_hi", [P, 4, HALVES, TILE], F32R)
        act_lo = sb("act_lo", [P, 4, HALVES, TILE], F32R)
        y_t = sb("y_t", [P, GROUPS, P])
        out_sb = sb("out_sb", [P, GROUPS, P])

        h_ps = ctx.enter_context(nc.psum_tensor("h_ps", [P, 2, HALVES, TILE], F32))
        y_ps = ctx.enter_context(nc.psum_tensor("y_ps", [P, TILE], F32))
        bank = [ctx.enter_context(nc.psum_tensor(f"bank{i}", [P, TILE], F32)) for i in range(3)]

        first_loaded = sem("first_loaded")
        w1_loaded, w2_loaded, wg_loaded = sem("w1_loaded"), sem("w2_loaded"), sem("wg_loaded")
        hi_split, lo_split = sem("hi_split"), sem("lo_split")
        zeroed = sem("zeroed")
        x_loaded = [sem(f"x_loaded{i}") for i in range(2)]
        ln_step = sem("ln_step")
        variance_ready = sem("variance_ready")
        rstd_ready = sem("rstd_ready")
        xn1_ready = sem("xn1_ready")
        t1_done = sem("t1_done")
        xn1_t_ready = sem("xn1_t_ready")
        q_done, k_done, v_done, kt_done = sem("q_done"), sem("k_done"), sem("v_done"), sem("kt_done")
        q_m_ready = sem("q_m_ready")
        q_d_ready = sem("q_d_ready")
        k_t_ready = sem("k_t_ready")
        k_d_ready = sem("k_d_ready")
        v_z_ready = sem("v_z_ready")
        qk_done = sem("qk_done")
        attn_ready = sem("attn_ready")
        u_done = sem("u_done")
        state_step = sem("state_step")
        state_ready = sem("state_ready")
        av_done = sem("av_done")
        o_t_ready = sem("o_t_ready")
        wo_done = sem("wo_done")
        x2_ready = sem("x2_ready")
        xn2_ready = sem("xn2_ready")
        t2_done = sem("t2_done")
        x_hi_ready = sem("x_hi_ready")
        x_lo_ready = sem("x_lo_ready")
        router_done = sem("router_done")
        top_ready = sem("top_ready")
        logits_ready = sem("logits_ready")
        expd_ready = sem("expd_ready")
        router_step = sem("router_step")
        combine_ready = sem("combine_ready")
        root_ready = sem("root_ready")
        root_t_done = sem("root_t_done")
        root_t_ready = sem("root_t_ready")
        root_stored = sem("root_stored")
        scale_loaded = [[sem(f"scale_loaded{i}{j}") for j in range(2)] for i in range(2)]
        h_done = sem("h_done")
        act_s_ready = sem("act_s_ready")
        act_hi_ready = sem("act_hi_ready")
        act_f_ready = sem("act_f_ready")
        act_lo_ready = sem("act_lo_ready")
        y_done = sem("y_done")
        y_t_ready = sem("y_t_ready")
        yt_done = sem("yt_done")
        out_ready = sem("out_ready")
        out_free = sem("out_free")

        passed = {e.engine: sem(f"passed_{n}") for n, e in
                  (("sp", nc.sync), ("pe", nc.tensor), ("dve", nc.vector))}

        LN_STEPS = 2 * (GROUPS + 1)
        ROUTER_STEPS = 10

        ident = cst[:, C_IDENT:C_IDENT + P]

        def wait_apart(eng, semaphore, value):
            eng.wait_ge(semaphore, value)
            eng.sem_inc(passed[eng.engine], 1)

        def chunk_of(ap, c):
            return ap[..., CHUNK * c:CHUNK * (c + 1)]

        def ring(t, e, n):
            return (EXPERTS * t.parity + e) % n

        def steps(eng, run):
            run(NONE, tile(0))
            run(tile(0), tile(1))
            if LOOP:
                with eng.Fori(0, (tiles - 2) // 2) as pair:
                    run(Tile(pair, 1, 1), Tile(pair, 2, 2))
                    run(Tile(pair, 2, 2), Tile(pair, 3, 3))
            else:
                for n in range(1, tiles - 1):
                    run(tile(n), tile(n + 1))
            run(tile(tiles - 1), NONE)
            run(tile(tiles), NONE)

        block = ctx.enter_context(nc.Block())

        @block.sync
        def _(sp):
            sp.dma_start(x_in[:, 0], x_t[0]).then_inc(x_loaded[0], DMA)
            sp.dma_start(cst[:], constants).then_inc(first_loaded, DMA)
            for n, w in enumerate((wq, wk, wv, wo)):
                sp.dma_start(w_attn[:, n], w).then_inc(first_loaded, DMA)
            sp.dma_start(x_in[:, 1], x_t[1]).then_inc(x_loaded[1], DMA)
            sp.sem_inc(out_free, DMA)

            def scales(t):
                wait_apart(sp, root_t_ready, t.count(1))
                if t.back(2).exists:
                    for j in range(2):
                        sp.wait_ge(scale_loaded[t.parity][j], t.back(2).count2(DMA))
                sp.dma_start(scratch[t.parity].rearrange("(r p) -> r p", p=P), combine_t[:]).then_inc(root_stored, DMA)
                wait_apart(sp, root_stored, t.count(DMA))
                if t.back(2).exists:
                    sp.wait_ge(act_s_ready, t.back(2).count(EXPERTS))
                for j in range(2):
                    half = slice(j * row // 2, (j + 1) * row // 2)
                    sp.dma_start(scale[:, t.parity].rearrange("p e n -> p (e n)")[:, half],
                                 scratch[t.parity, half].partition_broadcast(P)).then_inc(scale_loaded[t.parity][j], DMA)

            def load(t):
                wait_apart(sp, x2_ready, t.back(2).count(1))
                sp.dma_start(x_in[:, t.parity], x_t[bass.ds(t.index, 1)].rearrange("a p g d -> p (a g) d")
                             ).then_inc(x_loaded[t.parity], DMA)

            def store(t):
                wait_apart(sp, out_ready, t.count(1))
                sp.dma_start(out_t[bass.ds(t.index, 1)].rearrange("a p g d -> p (a g) d"), out_sb[:]
                             ).then_inc(out_free, DMA)

            scales(tile(0))
            load(tile(2))
            scales(tile(1))
            load(tile(3))

            def both(t):
                store(t.back(2))
                scales(t)
                load(Tile(t.pair, t.k + 2, t.first + 2))

            if LOOP:
                with sp.Fori(1, tiles // 2 - 1) as pair:
                    both(Tile(pair, 0, 2))
                    both(Tile(pair, 1, 3))
            else:
                for n in range(2, tiles - 2):
                    both(tile(n))
            for n in range(tiles - 2, tiles):
                store(tile(n - 2))
                scales(tile(n))
            store(tile(tiles - 2))
            store(tile(tiles - 1))
            sp.wait_ge(out_free, DMA * (tiles + 1))

        @block.tensor
        def _(pe):
            def w1_product(t, e):
                if e == 0:
                    pe.wait_ge(x_hi_ready, t.count(1))
                    pe.wait_ge(x_lo_ready, t.count(1))
                    if t.first == 0:
                        pe.wait_ge(hi_split, 3)
                        pe.wait_ge(lo_split, 3)
                if EXPERTS * t.first + e >= 2:
                    pe.wait_ge(act_s_ready, t.count(EXPERTS, e - 1))
                for half in range(HALVES):
                    cols = slice(half * P, (half + 1) * P)
                    h = h_ps[:, ring(t, e, 2), half]
                    pe.matmul(h, w1_lo[:, e, cols], x_hi[:, t.parity], start=True, stop=False)
                    pe.matmul(h, w1_hi[:, e, cols], x_lo[:, t.parity], start=False, stop=False)
                    last = pe.matmul(h, w1_hi[:, e, cols], x_hi[:, t.parity], start=False, stop=True)
                last.then_inc(h_done, 1)

            def w2_product(t, e):
                if not t.exists:
                    return
                if e == 0 and t.back(1).exists:
                    pe.wait_ge(y_t_ready, t.back(1).count(1))
                pe.wait_ge(act_hi_ready, t.count(EXPERTS, e + 1))
                r = ring(t, e, 4)
                for half in range(HALVES):
                    pe.matmul(y_ps[:], w2_lo[:, HALVES * e + half], act_hi[:, r, half],
                              start=(e == 0 and half == 0), stop=False)
                    pe.matmul(y_ps[:], w2_hi[:, HALVES * e + half], act_hi[:, r, half], start=False, stop=False)
                pe.wait_ge(act_lo_ready, t.count(HALVES * EXPERTS, HALVES * (e + 1)))
                for half in range(HALVES):
                    last = pe.matmul(y_ps[:], w2_hi[:, HALVES * e + half], act_lo[:, r, half], start=False,
                                     stop=(e == EXPERTS - 1 and half == HALVES - 1))
                last.then_inc(y_done, 1)

            def transpose_xn1(a):
                if a.back(1).exists:
                    pe.wait_ge(x_hi_ready, a.back(1).count(1))
                    pe.wait_ge(x_lo_ready, a.back(1).count(1))
                pe.wait_ge(xn1_ready, a.count(1))
                for g in range(GROUPS):
                    last = pe.transpose(bank[0][:, P * g:P * (g + 1)], xn1[:, g], ident)
                last.then_inc(t1_done, 1)

            def project_qk(a):
                pe.wait_ge(xn1_t_ready, a.count(1))
                if a.back(1).exists:
                    pe.wait_ge(logits_ready, a.back(1).count(1))
                pe.matmul(bank[1][:], w_attn[:, 0], xn1_t[:], start=True, stop=True).then_inc(q_done, 1)
                if a.back(1).exists:
                    pe.wait_ge(root_t_ready, a.back(1).count(1))
                pe.matmul(bank[2][:], w_attn[:, 1], xn1_t[:], start=True, stop=True).then_inc(k_done, 1)

            def project_v(a):
                for g in range(GROUPS):
                    last = pe.matmul(bank[0][:, P * g:P * (g + 1)], xn1_t[:, P * g:P * (g + 1)], w_attn[:, 2],
                                     start=True, stop=True)
                last.then_inc(v_done, 1)

            def transpose_k(a):
                pe.wait_ge(k_t_ready, a.count(1))
                pe.wait_ge(q_d_ready, a.count(1))
                for g in range(GROUPS):
                    last = pe.transpose(bank[1][:, P * g:P * (g + 1)], k_t[:, P * g:P * (g + 1)], ident)
                last.then_inc(kt_done, 1)

            def scores(a, pair):
                if pair == 1:
                    pe.wait_ge(v_z_ready, a.count(1))
                if pair >= 2:
                    pe.wait_ge(attn_ready, a.count(PAIRS, pair - 1))
                b = bank[2 if pair % 2 == 0 else 0]
                rows = slice(PW * pair, PW * (pair + 1))
                for g in range(GROUPS):
                    for c in range(2):
                        last = pe.matmul(b[CHUNK * c:CHUNK * (c + 1), P * g:P * (g + 1)],
                                         chunk_of(k_t[rows], 2 * g + c), chunk_of(q_m[rows], 2 * g + c),
                                         start=(g == 0), stop=(g == GROUPS - 1), skip_group_check=True)
                last.then_inc(qk_done, 1)

            def state_updates(a, p):
                pe.wait_ge(k_d_ready, a.count(1))
                if p.exists:
                    pe.wait_ge(out_ready, p.count(1))
                wait_apart(pe, attn_ready, a.count(PAIRS, 3))
                for g in range(GROUPS):
                    for pair in range(PAIRS):
                        for c in range(2):
                            rows = slice(CHUNK * c, CHUNK * (c + 1))
                            cols = slice(PW * pair, PW * (pair + 1))
                            last = pe.matmul(bank[1 + c][cols, PW * g:PW * (g + 1)], k_d[rows, g, cols],
                                             v_z[rows, PAIRS * g + pair, ::3], start=(g == 0),
                                             stop=(g == GROUPS - 1), skip_group_check=True)
                last.then_inc(u_done, 1)

            def outputs(a):
                wait_apart(pe, attn_ready, a.count(PAIRS))
                for g in range(GROUPS):
                    for j in range(2):
                        for pair in range(PAIRS):
                            for c in range(2):
                                if g + j + pair == 0 and c == 1:
                                    wait_apart(pe, state_ready, a.count(1))
                                rows = slice(CHUNK * c, CHUNK * (c + 1))
                                pe.matmul(bank[c][PW * pair:PW * (pair + 1), CHUNK * g:CHUNK * (g + 1)],
                                          v_z[rows, PAIRS * g + pair, 2 * j:2 * j + 2], attn[rows, pair, g, j],
                                          start=(g == 0 and j == 0), stop=False, skip_group_check=True)
                for g in range(GROUPS):
                    for c in range(2):
                        for pair in range(PAIRS):
                            rows = slice(PW * pair, PW * (pair + 1))
                            last = pe.matmul(bank[c][rows, CHUNK * g:CHUNK * (g + 1)], state_m[rows, 2 * g + c],
                                             chunk_of(q_d[rows], 2 * g + c), start=False,
                                             stop=(g == GROUPS - 1), skip_group_check=True)
                last.then_inc(av_done, 1)

            def project_out(a):
                pe.wait_ge(o_t_ready, a.count(1))
                for g in range(GROUPS):
                    last = pe.matmul(bank[2][:, P * g:P * (g + 1)], o_t[:, g], w_attn[:, 3], start=True, stop=True)
                last.then_inc(wo_done, 1)

            def transpose_xn2(a):
                pe.wait_ge(xn2_ready, a.count(1))
                for g in range(GROUPS):
                    last = pe.transpose(bank[0][:, P * g:P * (g + 1)], xn2[:, g], ident)
                last.then_inc(t2_done, 1)

            def route(a):
                if a.first == 0:
                    pe.wait_ge(hi_split, 2)
                    pe.wait_ge(lo_split, 2)
                pe.wait_ge(x_hi_ready, a.count(1))
                pe.wait_ge(x_lo_ready, a.count(1))
                for g in range(GROUPS):
                    o = bank[1][:, EXPERTS * g:EXPERTS * (g + 1)]
                    hi, lo = (part[:, a.parity, P * g:P * (g + 1)] for part in (x_hi, x_lo))
                    pe.matmul(o, lo, wg_hi[:], start=True, stop=False)
                    pe.matmul(o, hi, wg_lo[:], start=False, stop=False)
                    last = pe.matmul(o, hi, wg_hi[:], start=False, stop=True)
                last.then_inc(router_done, 1)

            def transpose_roots(a):
                pe.wait_ge(x2_ready, a.count(1))
                pe.wait_ge(root_ready, a.count(1))
                pe.transpose(bank[2][0:EXPERTS * GROUPS, 0:P], combine_r[:].rearrange("p e g -> p (e g)"), ident
                             ).then_inc(root_t_done, 1)

            def transpose_y(p, a):
                if not p.exists:
                    return
                if a.exists:
                    pe.wait_ge(k_d_ready, a.count(1))
                elif p.first == tiles - 2:
                    pe.wait_ge(logits_ready, tiles)
                else:
                    pe.wait_ge(out_ready, p.back(1).count(1))
                pe.wait_ge(y_t_ready, p.count(1))
                for g in range(GROUPS):
                    last = pe.transpose(bank[1][:, P * g:P * (g + 1)], y_t[:, g], ident)
                last.then_inc(yt_done, 1)

            def run(f, a):
                p = f.back(1)
                on = f.exists and f.first < tiles

                def w1(e):
                    if on:
                        w1_product(f, e)

                def w2(e):
                    if e < 0:
                        w2_product(p, EXPERTS + e)
                    elif on:
                        w2_product(f, e)

                w1(0)
                w2(-2)
                if a.exists:
                    transpose_xn1(a)
                w1(1)
                if a.exists:
                    project_qk(a)
                w2(-1)
                if a.exists:
                    project_v(a)
                    transpose_k(a)
                    scores(a, 0)
                    scores(a, 1)
                w1(2)
                transpose_y(p, a)
                if a.exists:
                    scores(a, 2)
                w2(0)
                if a.exists:
                    scores(a, 3)
                    state_updates(a, p)
                w1(3)
                w2(1)
                if a.exists:
                    outputs(a)
                w1(4)
                if a.exists:
                    project_out(a)
                w2(2)
                w1(5)
                w2(3)
                if a.exists:
                    transpose_xn2(a)
                w1(6)
                if a.exists:
                    route(a)
                w2(4)
                w1(7)
                w2(5)
                if a.exists:
                    transpose_roots(a)

            pe.wait_ge(first_loaded, 5 * DMA)
            steps(pe, run)

        @block.vector
        def _(dve):
            def norm_statistics(t, which, source):
                for g in range(GROUPS):
                    nc.vector.bn_stats(stats[:, which, g], source[:, g]).then_inc(ln_step, 1)
                wait_apart(dve, ln_step, t.count(LN_STEPS, which * (GROUPS + 1) + GROUPS))
                for g in range(GROUPS):
                    last = nc.vector.bn_aggr(moments[:, which, g], stats[:, which, g])
                last.then_inc(ln_step, 1)
                dve.wait_ge(ln_step, t.count(LN_STEPS, (which + 1) * (GROUPS + 1)))
                nc.vector.tensor_scalar(variance[:, which], moments[:, which, :, 1], LN_EPS, None, ALU.add
                                        ).then_inc(variance_ready, 1)

            def normalise(t, which, source, target, ready):
                dve.wait_ge(rstd_ready, t.count(2, which + 1))
                for g in range(GROUPS):
                    last = nc.vector.tensor_scalar(target[:, g], source[:, g], moments[:, which, g, 0:1],
                                                   rstd[:, which, g:g + 1], ALU.subtract, ALU.mult)
                last.then_inc(ready, 1)

            def scale_h(t, e):
                if not t.exists:
                    return
                if e % (EXPERTS // 2) == 0:
                    dve.wait_ge(scale_loaded[t.parity][e // (EXPERTS // 2)], t.count2(DMA))
                dve.wait_ge(h_done, t.count(EXPERTS, e + 1))
                if EXPERTS * t.first + e >= 2:
                    dve.wait_ge(act_f_ready, t.count(EXPERTS, e - 1))
                nc.vector.scalar_tensor_tensor(
                    out=act_s[:, ring(t, e, 2)], in0=h_ps[:, ring(t, e, 2)], scalar=0.0,
                    in1=scale[:, t.parity, e].unsqueeze(1).to_broadcast([P, HALVES, TILE]),
                    op0=ALU.max, op1=ALU.mult).then_inc(act_s_ready, 1)

            def decay_q(a):
                dve.wait_ge(q_m_ready, a.count(1))
                if a.back(1).exists:
                    dve.wait_ge(av_done, a.back(1).count(1))
                nc.vector.tensor_tensor(
                    q_d[:].rearrange("p (c i) -> p c i", i=CHUNK), bank[1][:].rearrange("p (c i) -> p c i", i=CHUNK),
                    cst[:, C_DQ:C_DQ + CHUNK].unsqueeze(1).to_broadcast([P, CHUNKS, CHUNK]), ALU.mult
                ).then_inc(q_d_ready, 1)

            def copy_v(a):
                dve.wait_ge(v_done, a.count(1))
                nc.vector.tensor_copy(v_z[:, :, ::3], bank[0][:].rearrange("p (n h d) -> p n h d", h=2, d=DH)
                                      ).then_inc(v_z_ready, 1)

            def decay_k(a):
                dve.wait_ge(kt_done, a.count(1))
                nc.vector.tensor_tensor(
                    k_d[:], bank[1][:].rearrange("p (g d) -> p g d", d=P),
                    cst[:, C_DK:C_DK + P].unsqueeze(1).to_broadcast([P, GROUPS, P]), ALU.mult
                ).then_inc(k_d_ready, 1)

            def decay_scores(a, pair):
                dve.wait_ge(qk_done, a.count(PAIRS, pair + 1))
                table = cst[:, C_DECAY + P * pair:C_DECAY + P * (pair + 1)]
                nc.vector.tensor_tensor(
                    attn[:, pair].rearrange("p g j i -> p g (j i)"),
                    bank[2 if pair % 2 == 0 else 0][:].rearrange("p (g n) -> p g n", n=P),
                    table.unsqueeze(1).to_broadcast([P, GROUPS, P]), ALU.mult).then_inc(attn_ready, 1)

            def scan_states(a):
                if a.back(1).exists:
                    dve.wait_ge(state_step, a.back(1).count(CHUNKS + 1))
                else:
                    dve.wait_ge(zeroed, 2)
                nc.vector.tensor_scalar(state[:, 0], state[:, CHUNKS], cst[:, bass.ds(a.index + C_LOW, 1)],
                                        cst[:, bass.ds(a.index + C_HIGH, 1)], ALU.max, ALU.min
                                        ).then_inc(state_step, 1)
                dve.wait_ge(u_done, a.count(1))
                for c in range(CHUNKS):
                    dve.wait_ge(state_step, a.count(CHUNKS + 1, c + 1))
                    nc.vector.scalar_tensor_tensor(
                        out=state[:, c + 1], in0=state[:, c], scalar=cst[:, C_DS:C_DS + 1],
                        in1=bank[1 + c % 2][:, PW * (c // 2):PW * (c // 2 + 1)], op0=ALU.mult, op1=ALU.add
                    ).then_inc(state_step, 1)
                dve.wait_ge(state_step, a.count(CHUNKS + 1))
                nc.vector.tensor_tensor(
                    state_m[:], state[:, 0:CHUNKS],
                    cst[:, C_SMASK:C_SMASK + PW].unsqueeze(1).to_broadcast([P, CHUNKS, PW]), ALU.mult
                ).then_inc(state_ready, 1)

            def add_attention(a):
                dve.wait_ge(wo_done, a.count(1))
                nc.vector.tensor_tensor(x2[:, a.parity], bank[2][:].rearrange("p (g d) -> p g d", d=P),
                                        x_in[:, a.parity], ALU.add).then_inc(x2_ready, 1)
                dve.wait_ge(x2_ready, a.count(1))

            def low_x(a):
                dve.wait_ge(x_hi_ready, a.count(1))
                nc.vector.tensor_tensor(x_lo[:, a.parity], bank[0][:], x_hi[:, a.parity].bitcast(F32), ALU.subtract
                                        ).then_inc(x_lo_ready, 1)

            def shift_logits(a):
                dve.wait_ge(router_done, a.count(1))
                l_ps = bank[1][:, 0:GROUPS * EXPERTS].rearrange("p (g e) -> p g e", e=EXPERTS)
                nc.vector.tensor_reduce(top[:], l_ps, AX_X, ALU.max).then_inc(top_ready, 1)
                dve.wait_ge(top_ready, a.count(1))
                nc.vector.tensor_tensor(logits[:], l_ps, top[:].unsqueeze(2).to_broadcast([P, GROUPS, EXPERTS]),
                                        ALU.subtract).then_inc(logits_ready, 1)

            def choose(a):
                done = [0]

                def step(ins):
                    ins.then_inc(router_step, 1)
                    done[0] += 1

                def after(n):
                    dve.wait_ge(router_step, a.count(ROUTER_STEPS, n))

                def by_expert(ap):
                    return ap.unsqueeze(2).to_broadcast([P, GROUPS, EXPERTS])

                iota = cst[:, C_IOTA:C_IOTA + EXPERTS].unsqueeze(1).to_broadcast([P, GROUPS, EXPERTS])
                dve.wait_ge(expd_ready, a.count(1))
                step(nc.vector.tensor_reduce(total[:], expd[:], AX_X, ALU.add))
                for g in range(GROUPS):
                    last = nc.vector.max(best[:, g], expd[:, g])
                step(last)
                after(2)
                step(nc.vector.scalar_tensor_tensor(out=denom[:, 0], in0=total[:], scalar=TOP_EPS,
                                                    in1=best[:, :, 0], op0=ALU.mult, op1=ALU.add))
                for g in range(GROUPS):
                    last = nc.vector.max_index(best_at[:, g], best[:, g], expd[:, g])
                step(last)
                after(3)
                step(nc.vector.tensor_tensor(denom[:, 1], denom[:, 0], best[:, :, 1], ALU.add))
                after(4)
                step(nc.vector.tensor_copy(best_f[:], best_at[:, :, 0:2]))
                after(6)
                nc.vector.tensor_tensor(chosen[:, 0], iota, by_expert(best_f[:, :, 0]), ALU.is_equal)
                step(nc.vector.tensor_tensor(chosen[:, 1], iota, by_expert(best_f[:, :, 1]), ALU.is_equal))
                step(nc.vector.reciprocal(r_denom[:], denom[:, 1]))
                after(7)
                step(nc.vector.tensor_tensor(chosen[:, 2], chosen[:, 0], chosen[:, 1], ALU.add))
                after(9)
                step(nc.vector.tensor_tensor(share[:], expd[:], chosen[:, 2], ALU.mult))
                after(10)
                if a.back(1).exists:
                    dve.wait_ge(root_ready, a.back(1).count(1))
                nc.vector.tensor_tensor(combine[:].rearrange("p e g -> p g e"), share[:], by_expert(r_denom[:]),
                                        ALU.mult).then_inc(combine_ready, 1)
                assert done[0] == ROUTER_STEPS

            def add_experts(p):
                if not p.exists:
                    return
                dve.wait_ge(yt_done, p.count(1))
                dve.wait_ge(out_free, p.count(DMA))
                nc.vector.tensor_tensor(out_sb[:], bank[1][:].rearrange("p (g d) -> p g d", d=P), x2[:, p.parity],
                                        ALU.add).then_inc(out_ready, 1)

            def run(f, a):
                p = f.back(1)
                on = f.exists and f.first < tiles

                def h(e):
                    if e < 0:
                        scale_h(p, EXPERTS + e)
                    elif on:
                        scale_h(f, e)

                if a.exists:
                    dve.wait_ge(x_loaded[a.parity], a.count2(DMA))
                    norm_statistics(a, 0, x_in[:, a.parity])
                h(-1)
                if a.exists:
                    normalise(a, 0, x_in[:, a.parity], xn1, xn1_ready)
                    decay_q(a)
                    copy_v(a)
                    decay_k(a)
                h(0)
                if a.exists:
                    decay_scores(a, 0)
                    decay_scores(a, 1)
                h(1)
                add_experts(p)
                if a.exists:
                    decay_scores(a, 2)
                    decay_scores(a, 3)
                    scan_states(a)
                h(2)
                h(3)
                if a.exists:
                    add_attention(a)
                    norm_statistics(a, 1, x2[:, a.parity])
                h(4)
                if a.exists:
                    normalise(a, 1, x2[:, a.parity], xn2, xn2_ready)
                h(5)
                if a.exists:
                    low_x(a)
                    shift_logits(a)
                    choose(a)
                h(6)

            nc.vector.memset(v_z[:], 0.0).then_inc(zeroed, 1)
            nc.vector.memset(state[:, CHUNKS], 0.0).then_inc(zeroed, 1)
            dve.wait_ge(first_loaded, 5 * DMA)
            dve.wait_ge(zeroed, 2)
            steps(dve, run)

        @block.scalar
        def _(act):
            act.dma_start(wg_in[:], wg).then_inc(wg_loaded, DMA)
            act.dma_start(w1_in[:], w1.rearrange("e d h -> d e h")).then_inc(w1_loaded, DMA)
            act.dma_start(w2_in[:], w2.rearrange("e (n h) d -> h (e n) d", h=P)).then_inc(w2_loaded, DMA)

            def square(t, e):
                if not t.exists:
                    return
                act.wait_ge(act_s_ready, t.count(EXPERTS, e + 1))
                if EXPERTS * t.first + e >= 4:
                    act.wait_ge(y_done, t.count(EXPERTS, e - 3))
                nc.scalar.activation(act_hi[:, ring(t, e, 4)], act_s[:, ring(t, e, 2)], ACT.Square
                                     ).then_inc(act_hi_ready, 1)
                if EXPERTS * t.first + e >= 2:
                    act.wait_ge(act_lo_ready, t.count(HALVES * EXPERTS, HALVES * (e - 1)))
                nc.scalar.activation(act_f[:, ring(t, e, 2)], act_s[:, ring(t, e, 2)], ACT.Square
                                     ).then_inc(act_f_ready, 1)

            def copy_xn1(a):
                act.wait_ge(t1_done, a.count(1))
                if a.back(1).exists:
                    act.wait_ge(v_done, a.back(1).count(1))
                nc.scalar.copy(xn1_t[:], bank[0][:]).then_inc(xn1_t_ready, 1)

            def mask_q(a):
                act.wait_ge(q_done, a.count(1))
                nc.scalar.activation(q_m[:, 0], bank[1][:], ACT.Copy, scale=cst[:, C_EVEN:C_EVEN + 1])
                nc.scalar.activation(q_m[:, 1], bank[1][:], ACT.Copy, scale=cst[:, C_ODD:C_ODD + 1]
                                     ).then_inc(q_m_ready, 1)

            def copy_k(a):
                act.wait_ge(k_done, a.count(1))
                nc.scalar.copy(k_t[:], bank[2][:]).then_inc(k_t_ready, 1)

            def copy_y(p):
                if not p.exists:
                    return
                act.wait_ge(y_done, p.count(EXPERTS))
                if p.back(1).exists:
                    act.wait_ge(yt_done, p.back(1).count(1))
                nc.scalar.copy(y_t[:].rearrange("p g n -> p (g n)"), y_ps[:]).then_inc(y_t_ready, 1)

            def copy_o(a):
                act.wait_ge(av_done, a.count(1))
                for c in range(2):
                    last = nc.scalar.copy(o_t[:, :, c], bank[c][:, 0:TILE // 2].rearrange("p (g i) -> p g i", i=CHUNK))
                last.then_inc(o_t_ready, 1)

            def high_x(a):
                act.wait_ge(t2_done, a.count(1))
                if a.back(2).exists:
                    act.wait_ge(h_done, a.back(2).count(EXPERTS))
                nc.scalar.copy(x_hi[:, a.parity], bank[0][:]).then_inc(x_hi_ready, 1)

            def exponentiate(a):
                act.wait_ge(logits_ready, a.count(1))
                nc.scalar.activation(expd[:], logits[:], ACT.Exp).then_inc(expd_ready, 1)

            def copy_roots(a):
                act.wait_ge(root_t_done, a.count(1))
                if a.back(1).exists:
                    act.wait_ge(root_stored, a.back(1).count(DMA))
                nc.scalar.copy(combine_t[:], bank[2][0:EXPERTS * GROUPS, 0:P]).then_inc(root_t_ready, 1)

            def run(f, a):
                p = f.back(1)
                on = f.exists and f.first < tiles
                start = a.exists and a.first == 0

                def s(e):
                    if e < 0:
                        square(p, EXPERTS + e)
                    elif on:
                        square(f, e)

                if a.exists:
                    copy_xn1(a)
                s(-1)
                if a.exists:
                    mask_q(a)
                    copy_k(a)
                copy_y(p)
                s(0)
                if start:
                    act.wait_ge(w1_loaded, DMA)
                    nc.scalar.copy(w1_hi[:], w1_in[:]).then_inc(hi_split, 1)
                    act.wait_ge(wg_loaded, DMA)
                    nc.scalar.copy(wg_hi[:], wg_in[:]).then_inc(hi_split, 1)
                s(1)
                s(2)
                if a.exists:
                    copy_o(a)
                if start:
                    act.wait_ge(w2_loaded, DMA)
                    nc.scalar.copy(w2_hi[:], w2_in[:]).then_inc(hi_split, 1)
                s(3)
                s(4)
                if a.exists:
                    high_x(a)
                s(5)
                if a.exists:
                    exponentiate(a)
                s(6)
                if a.exists:
                    copy_roots(a)

            act.wait_ge(first_loaded, 5 * DMA)
            steps(act, run)

        @block.gpsimd
        def _(pool):
            def low(t, e):
                if not t.exists:
                    return
                pool.wait_ge(act_f_ready, t.count(EXPERTS, e + 1))
                if EXPERTS * t.first + e >= 4:
                    pool.wait_ge(y_done, t.count(EXPERTS, e - 3))
                for half in range(HALVES):
                    nc.gpsimd.tensor_tensor(act_lo[:, ring(t, e, 4), half], act_f[:, ring(t, e, 2), half],
                                            act_hi[:, ring(t, e, 4), half].bitcast(F32), ALU.subtract
                                            ).then_inc(act_lo_ready, 1)

            def root(t, which):
                pool.wait_ge(variance_ready, t.count(2, which + 1))
                nc.gpsimd.tensor_tensor(rstd[:, which], variance[:, which], cst[:, C_MHALF:C_MHALF + GROUPS], ALU.pow
                                        ).then_inc(rstd_ready, 1)

            def split(hi, lo, whole, n):
                pool.wait_ge(hi_split, n)
                nc.gpsimd.tensor_tensor(lo[:], whole[:], hi[:].bitcast(F32), ALU.subtract).then_inc(lo_split, 1)

            def run(f, a):
                p = f.back(1)
                on = f.exists and f.first < tiles
                start = a.exists and a.first == 0

                def lo(e):
                    if e < 0:
                        low(p, EXPERTS + e)
                    elif on:
                        low(f, e)

                if a.exists:
                    root(a, 0)
                lo(-1)
                if start:
                    split(w1_hi, w1_lo, w1_in, 1)
                    split(wg_hi, wg_lo, wg_in, 2)
                for e in range(4):
                    lo(e)
                if a.exists:
                    root(a, 1)
                if start:
                    split(w2_hi, w2_lo, w2_in, 3)
                lo(4)
                lo(5)
                if a.exists:
                    pool.wait_ge(combine_ready, a.count(1))
                    if a.back(1).exists:
                        pool.wait_ge(root_t_done, a.back(1).count(1))
                    nc.gpsimd.tensor_tensor(
                        combine_r[:].rearrange("p e g -> p (e g)"), combine[:].rearrange("p e g -> p (e g)"),
                        cst[:, C_HALF:C_HALF + GROUPS * EXPERTS], ALU.pow).then_inc(root_ready, 1)
                lo(6)

            pool.wait_ge(first_loaded, 5 * DMA)
            steps(pool, run)


LOOP = True


def constant_table():
    import numpy as np

    gamma = 1.0 - np.exp2(-5.0 - np.arange(HEADS))
    i = np.arange(CHUNK)
    t = np.zeros((P, C_ALL), np.float64)
    t[:, C_IDENT:C_IDENT + P] = np.eye(P)
    diff = i[None, :] - i[:, None]
    decay = np.where(diff >= 0, gamma[:, None, None] ** np.maximum(diff, 0), 0.0) * DH ** -0.5
    t[:, C_DECAY:C_DECAY + HEADS * CHUNK] = np.tile(decay.transpose(1, 0, 2).reshape(CHUNK, -1), (2, 1))
    head = np.arange(P) // DH
    t[:, C_DQ:C_DQ + CHUNK] = gamma[head][:, None] ** (i[None, :] + 1) * DH ** -0.5
    t[:, C_DK:C_DK + P] = np.tile(gamma[head][None, :] ** (CHUNK - 1 - i[:, None]), (2, 1))
    t[:, C_EVEN] = head % 2 == 0
    t[:, C_ODD] = head % 2 == 1
    t[:, C_DS] = gamma[head] ** CHUNK
    t[:, C_SMASK:C_SMASK + PW] = (head % 2)[:, None] == (np.arange(PW) // DH)[None, :]
    fresh = np.arange(8) % 4 == 0
    t[:, C_LOW:C_LOW + 8] = np.where(fresh, 0.0, -BIG)
    t[:, C_HIGH:C_HIGH + 8] = np.where(fresh, 0.0, BIG)
    t[:, C_IOTA:C_IOTA + EXPERTS] = np.arange(EXPERTS)
    t[:, C_MHALF:C_MHALF + GROUPS] = -0.5
    t[:, C_HALF:C_HALF + GROUPS * EXPERTS] = 0.5
    return t.astype(np.float32)


def kernel(**inputs):
    import numpy as np
    import concourse.bacc as bacc
    from concourse.bass_utils import run_bass_kernel_spmd

    nc = bacc.Bacc("TRN2", target_bir_lowering=False, num_devices=1)
    names = {"x": "L0_attn_hidden_states", "wq": "L0_attn_Wq", "wk": "L0_attn_Wk", "wv": "L0_attn_Wv",
             "wo": "L0_attn_Wo", "wg": "L0_ffn_Wg", "w1": "L0_ffn_W1", "w2": "L0_ffn_W2"}
    arrays = {k: np.ascontiguousarray(inputs[n]) for k, n in names.items()}
    arrays["constants"] = constant_table()
    args = {k: nc.dram_tensor(k, a.shape, F32, kind="ExternalInput").ap() for k, a in arrays.items()}
    scratch = nc.dram_tensor("scratch", (2, EXPERTS * TILE), F32, kind="Internal").ap()
    out = nc.dram_tensor("out", arrays["x"].shape, F32, kind="ExternalOutput").ap()
    build(nc, scratch=scratch, out=out, **args)
    result = run_bass_kernel_spmd(nc, [arrays], core_ids=[0])
    return result.results[0]["out"]
```

```python
from contextlib import ExitStack

import concourse.bass as bass
from concourse import mybir

F32 = mybir.dt.float32
F32R = mybir.dt.float32r
U32 = mybir.dt.uint32
ALU = mybir.AluOpType
ACT = mybir.ActivationFunctionType
AX_X = mybir.AxisListType.X

P = 128
HEADS = 8
DH = P // HEADS
CHUNK = 64
PAIRS = HEADS // 2
PW = 2 * DH
TILE = 512
GROUPS = TILE // P
CHUNKS = TILE // CHUNK
EXPERTS = 8
HIDDEN = 256
HALVES = HIDDEN // P
LN_EPS = 1e-5
TOP_EPS = 1e-8
BIG = 3.4028234e38
PARTS = 4
DVE_ALONE = 2
DMA = 16

C_IDENT = 0
C_DECAY = C_IDENT + P
C_DQ = C_DECAY + HEADS * CHUNK
C_DK = C_DQ + CHUNK
C_EVEN = C_DK + P
C_ODD = C_EVEN + 1
C_DS = C_ODD + 1
C_SMASK = C_DS + 1
C_LOW = C_SMASK + PW
C_HIGH = C_LOW + 8
C_IOTA = C_HIGH + 8
C_ALL = C_IOTA + EXPERTS


class Tile:

    def __init__(self, pair, k, first):
        self.pair, self.k, self.first = pair, k, first
        self.index = pair * 2 + k
        self.parity = k % 2
        self.exists = first >= 0

    def back(self, n):
        return Tile(self.pair, self.k - n, self.first - n)

    def count(self, per_tile, n=None):
        return self.pair * (2 * per_tile) + (self.k * per_tile + (per_tile if n is None else n))

    def count2(self, per_tile):
        return self.pair * per_tile + (self.k // 2 + 1) * per_tile


def tile(n):
    return Tile(n // 2, n % 2, n)


NONE = Tile(0, -9, -9)


def build(nc, x, wq, wk, wv, wo, wg, w1, w2, constants, scratch, out):
    tokens = x.shape[0] * x.shape[1]
    tiles = tokens // TILE
    assert tiles == 8 and x.shape[2] == P
    x_t = x.rearrange("b (t g p) d -> (b t) p g d", g=GROUPS, p=P)
    out_t = out.rearrange("b (t g p) d -> (b t) p g d", g=GROUPS, p=P)
    row = EXPERTS * TILE

    with ExitStack() as ctx:
        def sb(name, shape, dt=F32):
            return ctx.enter_context(nc.sbuf_tensor(name, shape, dt))

        def sem(name):
            return ctx.enter_context(nc.semaphore(name))

        cst = sb("cst", [P, C_ALL])
        w_attn = sb("w_attn", [P, 4, P])
        wg_in = sb("wg_in", [P, EXPERTS])
        wg_hi, wg_lo = (sb(n, [P, EXPERTS], F32R) for n in ("wg_hi", "wg_lo"))
        w1_in = sb("w1_in", [P, EXPERTS, HIDDEN])
        w1_hi, w1_lo = (sb(n, [P, EXPERTS, HIDDEN], F32R) for n in ("w1_hi", "w1_lo"))
        w2_in = sb("w2_in", [P, EXPERTS * HALVES, P])
        w2_hi, w2_lo = (sb(n, [P, EXPERTS * HALVES, P], F32R) for n in ("w2_hi", "w2_lo"))

        x_in = sb("x_in", [P, 2, GROUPS, P])
        minus_half = sb("minus_half", [P, GROUPS])
        half = sb("half", [P, GROUPS * 2])
        stats = sb("stats", [P, 2, GROUPS, 6])
        moments = sb("moments", [P, 2, GROUPS, 2])
        variance = sb("variance", [P, 2, GROUPS])
        rstd = sb("rstd", [P, 2, GROUPS])
        xn1 = sb("xn1", [P, GROUPS, P])
        xn1_t = sb("xn1_t", [P, TILE])
        q_m = sb("q_m", [P, 2, TILE])
        q_d = sb("q_d", [P, TILE])
        k_t = sb("k_t", [P, TILE])
        k_d = sb("k_d", [P, GROUPS, P])
        v_z = sb("v_z", [P, GROUPS * PAIRS, 4, DH])
        attn = sb("attn", [P, PAIRS, GROUPS, 2, CHUNK])
        state = sb("state", [P, CHUNKS + 1, PW])
        state_m = sb("state_m", [P, CHUNKS, PW])
        o_t = sb("o_t", [P, GROUPS, 2, CHUNK])
        x2 = sb("x2", [P, 2, GROUPS, P])
        xn2 = sb("xn2", [P, GROUPS, P])
        x_hi = sb("x_hi", [P, 2, TILE], F32R)
        x_lo = sb("x_lo", [P, 2, TILE], F32R)
        top = sb("top", [P, GROUPS])
        logits = sb("logits", [P, GROUPS, EXPERTS])
        expd = sb("expd", [P, GROUPS, EXPERTS])
        total = sb("total", [P, GROUPS])
        best = sb("best", [P, GROUPS, 8])
        best_at = sb("best_at", [P, GROUPS, 8], U32)
        best_f = sb("best_f", [P, GROUPS, 2])
        denom = sb("denom", [P, 2, GROUPS])
        r_denom = sb("r_denom", [P, GROUPS])
        chosen = sb("chosen", [P, 2, GROUPS, EXPERTS])
        share = sb("share", [P, GROUPS, 2])
        root = sb("root", [P, GROUPS, 2])
        spread = sb("spread", [P, 2, GROUPS, EXPERTS])
        combine_r = sb("combine_r", [P, EXPERTS, GROUPS])
        combine_t = sb("combine_t", [EXPERTS * GROUPS, P])
        scale = sb("scale", [P, 2, EXPERTS, TILE])
        zeros = sb("zeros", [P, 256])
        table_load = sb("table_load", [P, 1])
        act_s = sb("act_s", [P, 2, HALVES, TILE])
        act_f = sb("act_f", [P, 2, HALVES, TILE])
        act_hi = sb("act_hi", [P, 4, HALVES, TILE], F32R)
        act_lo = sb("act_lo", [P, 4, HALVES, TILE], F32R)
        y_t = sb("y_t", [P, GROUPS, P])
        out_sb = sb("out_sb", [P, GROUPS, P])

        h_ps = ctx.enter_context(nc.psum_tensor("h_ps", [P, 2, HALVES, TILE], F32))
        y_ps = ctx.enter_context(nc.psum_tensor("y_ps", [P, TILE], F32))
        bank = [ctx.enter_context(nc.psum_tensor(f"bank{i}", [P, TILE], F32)) for i in range(3)]
        score_bank = (bank[0], bank[1], bank[2], bank[0])
        chunk_bank = (bank[1], bank[2])

        first_loaded = sem("first_loaded")
        w1_loaded, w2_loaded, wg_loaded = sem("w1_loaded"), sem("w2_loaded"), sem("wg_loaded")
        hi_split, lo_split = sem("hi_split"), sem("lo_split")
        zeroed = sem("zeroed")
        exponents_set = sem("exponents_set")
        x_loaded = [sem(f"x_loaded{i}") for i in range(2)]
        norm_step = [sem(f"norm_step{i}") for i in range(2)]
        variance_ready = [sem(f"variance_ready{i}") for i in range(2)]
        rstd_ready = [sem(f"rstd_ready{i}") for i in range(2)]
        xn1_ready = sem("xn1_ready")
        t1_done = sem("t1_done")
        xn1_t_ready = sem("xn1_t_ready")
        q_done, k_done, v_done, kt_done = sem("q_done"), sem("k_done"), sem("v_done"), sem("kt_done")
        q_m_ready = sem("q_m_ready")
        q_d_ready = sem("q_d_ready")
        k_t_ready = sem("k_t_ready")
        k_d_ready = sem("k_d_ready")
        v_z_ready = sem("v_z_ready")
        qk_done = sem("qk_done")
        attn_ready = sem("attn_ready")
        u_done = sem("u_done")
        state_step = sem("state_step")
        state_ready = sem("state_ready")
        av_done = sem("av_done")
        o_t_ready = sem("o_t_ready")
        wo_done = sem("wo_done")
        x2_ready = sem("x2_ready")
        xn2_ready = sem("xn2_ready")
        t2_done = sem("t2_done")
        x_hi_ready = sem("x_hi_ready")
        x_lo_ready = sem("x_lo_ready")
        router_done = sem("router_done")
        top_ready = sem("top_ready")
        logits_ready = sem("logits_ready")
        expd_ready = sem("expd_ready")
        router_step = sem("router_step")
        share_ready = sem("share_ready")
        combine_ready = sem("combine_ready")
        root_ready = sem("root_ready")
        root_t_done = sem("root_t_done")
        root_t_ready = sem("root_t_ready")
        root_stored = sem("root_stored")
        scale_loaded = [[sem(f"scale_loaded{i}{j}") for j in range(PARTS)] for i in range(2)]
        h_done = sem("h_done")
        act_s_ready = sem("act_s_ready")
        act_hi_ready = sem("act_hi_ready")
        act_f_ready = sem("act_f_ready")
        dve_low_ready = sem("dve_low_ready")
        y_done = sem("y_done")
        pool_low_ready = sem("pool_low_ready")
        y_t_ready = sem("y_t_ready")
        yt_done = sem("yt_done")
        out_ready = sem("out_ready")
        out_free = sem("out_free")

        passed = {e.engine: sem(f"passed_{n}") for n, e in
                  (("sp", nc.sync), ("pe", nc.tensor), ("dve", nc.vector))}

        ROUTER_STEPS = 9

        ident = cst[:, C_IDENT:C_IDENT + P]

        def wait_apart(eng, semaphore, value):
            eng.wait_ge(semaphore, value)
            eng.sem_inc(passed[eng.engine], 1)

        def chunk_of(ap, c):
            return ap[..., CHUNK * c:CHUNK * (c + 1)]

        def ring(t, e, n):
            return (EXPERTS * t.parity + e) % n

        def pool_lows(t, n):
            return t.count(EXPERTS - 1, n - (n > DVE_ALONE))

        def steps(eng, run):
            run(NONE, tile(0))
            run(tile(0), tile(1))
            with eng.Fori(0, (tiles - 2) // 2) as pair:
                run(Tile(pair, 1, 1), Tile(pair, 2, 2))
                run(Tile(pair, 2, 2), Tile(pair, 3, 3))
            run(tile(tiles - 1), NONE)
            run(tile(tiles), NONE)

        block = ctx.enter_context(nc.Block())

        @block.sync
        def _(sp):
            sp.dma_start(x_in[:, 0], x_t[0]).then_inc(x_loaded[0], DMA)
            sp.dma_start(cst[:], constants).then_inc(first_loaded, DMA)
            for n, w in enumerate((wq, wk, wv, wo)):
                sp.dma_start(w_attn[:, n], w).then_inc(first_loaded, DMA)
            sp.dma_start(x_in[:, 1], x_t[1]).then_inc(x_loaded[1], DMA)
            sp.sem_inc(out_free, DMA)

            def scales(t):
                wait_apart(sp, root_t_ready, t.count(1))
                if t.back(2).exists:
                    for j in range(PARTS):
                        sp.wait_ge(scale_loaded[t.parity][j], t.back(2).count2(DMA))
                sp.dma_start(scratch[t.parity].rearrange("(r p) -> r p", p=P), combine_t[:]).then_inc(root_stored, DMA)
                wait_apart(sp, root_stored, t.count(DMA))
                if t.back(2).exists:
                    sp.wait_ge(act_s_ready, t.back(2).count(EXPERTS))
                for j in range(PARTS):
                    part = slice(j * row // PARTS, (j + 1) * row // PARTS)
                    sp.dma_start(scale[:, t.parity].rearrange("p e n -> p (e n)")[:, part],
                                 scratch[t.parity, part].partition_broadcast(P)).then_inc(scale_loaded[t.parity][j], DMA)

            def load(t):
                wait_apart(sp, x2_ready, t.back(2).count(1))
                sp.dma_start(x_in[:, t.parity], x_t[bass.ds(t.index, 1)].rearrange("a p g d -> p (a g) d")
                             ).then_inc(x_loaded[t.parity], DMA)

            def store(t):
                wait_apart(sp, out_ready, t.count(1))
                sp.dma_start(out_t[bass.ds(t.index, 1)].rearrange("a p g d -> p (a g) d"), out_sb[:]
                             ).then_inc(out_free, DMA)

            def both(t):
                scales(t)
                load(Tile(t.pair, t.k + 2, t.first + 2))
                if t.back(1).exists:
                    store(t.back(1))

            both(tile(0))
            both(tile(1))
            with sp.Fori(1, tiles // 2 - 1) as pair:
                both(Tile(pair, 0, 2))
                both(Tile(pair, 1, 3))
            for n in range(tiles - 2, tiles):
                scales(tile(n))
                store(tile(n - 1))
            store(tile(tiles - 1))
            sp.wait_ge(out_free, DMA * (tiles + 1))

        @block.tensor
        def _(pe):
            def keep_warm(n):
                for _ in range(n):
                    pe.matmul(h_ps[:, 0, 0, 0:256], zeros[:, 0:P], zeros[:], start=True, stop=True)

            def w1_product(t, e):
                if e == 0:
                    pe.wait_ge(x_hi_ready, t.count(1))
                    pe.wait_ge(x_lo_ready, t.count(1))
                    if t.first == 0:
                        pe.wait_ge(hi_split, 3)
                        pe.wait_ge(lo_split, 3)
                if EXPERTS * t.first + e >= 2:
                    pe.wait_ge(act_s_ready, t.count(EXPERTS, e - 1))
                for half in range(HALVES):
                    cols = slice(half * P, (half + 1) * P)
                    h = h_ps[:, ring(t, e, 2), half]
                    pe.matmul(h, w1_lo[:, e, cols], x_hi[:, t.parity], start=True, stop=False)
                    pe.matmul(h, w1_hi[:, e, cols], x_lo[:, t.parity], start=False, stop=False)
                    last = pe.matmul(h, w1_hi[:, e, cols], x_hi[:, t.parity], start=False, stop=True)
                last.then_inc(h_done, 1)

            def w2_high(t, e):
                if e == 0 and t.back(1).exists:
                    pe.wait_ge(y_t_ready, t.back(1).count(1))
                pe.wait_ge(act_hi_ready, t.count(EXPERTS, e + 1))
                r = ring(t, e, 4)
                for half in range(HALVES):
                    pe.matmul(y_ps[:], w2_lo[:, HALVES * e + half], act_hi[:, r, half],
                              start=(e == 0 and half == 0), stop=False)
                    pe.matmul(y_ps[:], w2_hi[:, HALVES * e + half], act_hi[:, r, half], start=False, stop=False)

            def w2_low(t, e):
                r = ring(t, e, 4)
                pe.wait_ge(pool_low_ready, pool_lows(t, e + 1))
                pe.wait_ge(dve_low_ready, t.count(EXPERTS, e + 1))
                for half in range(HALVES):
                    last = pe.matmul(y_ps[:], w2_hi[:, HALVES * e + half], act_lo[:, r, half], start=False,
                                     stop=(e == EXPERTS - 1 and half == HALVES - 1))
                last.then_inc(y_done, 1)

            def transpose_xn1(a):
                if a.back(1).exists:
                    pe.wait_ge(x2_ready, a.back(1).count(1))
                pe.wait_ge(xn1_ready, a.count(1))
                for g in range(GROUPS):
                    last = pe.transpose(bank[0][:, P * g:P * (g + 1)], xn1[:, g], ident)
                last.then_inc(t1_done, 1)

            def project_qk(a):
                pe.wait_ge(xn1_t_ready, a.count(1))
                if a.back(1).exists:
                    pe.wait_ge(x_lo_ready, a.back(1).count(1))
                pe.matmul(bank[1][:], w_attn[:, 0], xn1_t[:], start=True, stop=True).then_inc(q_done, 1)
                if a.back(1).exists:
                    pe.wait_ge(logits_ready, a.back(1).count(1))
                pe.matmul(bank[2][:], w_attn[:, 1], xn1_t[:], start=True, stop=True).then_inc(k_done, 1)

            def project_v(a):
                for g in range(GROUPS):
                    last = pe.matmul(bank[0][:, P * g:P * (g + 1)], xn1_t[:, P * g:P * (g + 1)], w_attn[:, 2],
                                     start=True, stop=True)
                last.then_inc(v_done, 1)

            def transpose_k(a):
                pe.wait_ge(q_d_ready, a.count(1))
                pe.wait_ge(k_t_ready, a.count(1))
                for g in range(GROUPS):
                    last = pe.transpose(bank[1][:, P * g:P * (g + 1)], k_t[:, P * g:P * (g + 1)], ident)
                last.then_inc(kt_done, 1)

            def scores(a, pair, f):
                if pair == 0:
                    pe.wait_ge(v_z_ready, a.count(1))
                if pair == 1:
                    pe.wait_ge(k_d_ready, a.count(1))
                if pair == 2 and f.exists:
                    pe.wait_ge(root_t_ready, f.count(1))
                if pair == 3:
                    pe.wait_ge(attn_ready, a.count(PAIRS, 1))
                b = score_bank[pair]
                rows = slice(PW * pair, PW * (pair + 1))
                for g in range(GROUPS):
                    for c in range(2):
                        last = pe.matmul(b[CHUNK * c:CHUNK * (c + 1), P * g:P * (g + 1)],
                                         chunk_of(k_t[rows], 2 * g + c), chunk_of(q_m[rows], 2 * g + c),
                                         start=(g == 0), stop=(g == GROUPS - 1), skip_group_check=True)
                last.then_inc(qk_done, 1)

            def state_updates(a):
                wait_apart(pe, attn_ready, a.count(PAIRS, 3))
                for g in range(GROUPS):
                    for pair in range(PAIRS):
                        for c in range(2):
                            rows = slice(CHUNK * c, CHUNK * (c + 1))
                            cols = slice(PW * pair, PW * (pair + 1))
                            last = pe.matmul(chunk_bank[c][cols, PW * g:PW * (g + 1)], k_d[rows, g, cols],
                                             v_z[rows, PAIRS * g + pair, ::3], start=(g == 0),
                                             stop=(g == GROUPS - 1), skip_group_check=True)
                last.then_inc(u_done, 1)

            def outputs(a, groups):
                if 0 in groups:
                    pe.wait_ge(attn_ready, a.count(PAIRS))
                    wait_apart(pe, state_ready, a.count(1))
                for g in groups:
                    for j in range(2):
                        for pair in range(PAIRS):
                            for c in range(2):
                                rows = slice(CHUNK * c, CHUNK * (c + 1))
                                pe.matmul(chunk_bank[c][PW * pair:PW * (pair + 1), CHUNK * g:CHUNK * (g + 1)],
                                          v_z[rows, PAIRS * g + pair, 2 * j:2 * j + 2], attn[rows, pair, g, j],
                                          start=(g == 0 and j == 0), stop=False, skip_group_check=True)
                for g in groups:
                    for c in range(2):
                        for pair in range(PAIRS):
                            rows = slice(PW * pair, PW * (pair + 1))
                            last = pe.matmul(chunk_bank[c][rows, CHUNK * g:CHUNK * (g + 1)], state_m[rows, 2 * g + c],
                                             chunk_of(q_d[rows], 2 * g + c), start=False,
                                             stop=(g == GROUPS - 1), skip_group_check=True)
                if GROUPS - 1 in groups:
                    last.then_inc(av_done, 1)

            def project_out(a, p):
                if p.exists:
                    pe.wait_ge(out_ready, p.count(1))
                pe.wait_ge(o_t_ready, a.count(1))
                for g in range(GROUPS):
                    last = pe.matmul(bank[0][:, P * g:P * (g + 1)], o_t[:, g], w_attn[:, 3], start=True, stop=True)
                last.then_inc(wo_done, 1)

            def transpose_xn2(a):
                pe.wait_ge(xn2_ready, a.count(1))
                for g in range(GROUPS):
                    last = pe.transpose(bank[1][:, P * g:P * (g + 1)], xn2[:, g], ident)
                last.then_inc(t2_done, 1)

            def route(a):
                if a.first == 0:
                    pe.wait_ge(hi_split, 2)
                    pe.wait_ge(lo_split, 2)
                pe.wait_ge(x_hi_ready, a.count(1))
                pe.wait_ge(x_lo_ready, a.count(1))
                for g in range(GROUPS):
                    o = bank[2][:, EXPERTS * g:EXPERTS * (g + 1)]
                    hi, lo = (part[:, a.parity, P * g:P * (g + 1)] for part in (x_hi, x_lo))
                    pe.matmul(o, lo, wg_hi[:], start=True, stop=False)
                    pe.matmul(o, hi, wg_lo[:], start=False, stop=False)
                    last = pe.matmul(o, hi, wg_hi[:], start=False, stop=True)
                last.then_inc(router_done, 1)

            def transpose_roots(f):
                pe.wait_ge(combine_ready, f.count(1))
                pe.transpose(bank[2][0:EXPERTS * GROUPS, 0:P], combine_r[:].rearrange("p e g -> p (e g)"), ident
                             ).then_inc(root_t_done, 1)

            def transpose_y(p, a):
                if not p.exists:
                    return
                if a.exists:
                    pe.wait_ge(attn_ready, a.count(PAIRS))
                elif p.first == tiles - 2:
                    pe.wait_ge(x2_ready, tiles)
                else:
                    pe.wait_ge(out_ready, p.back(1).count(1))
                pe.wait_ge(y_t_ready, p.count(1))
                for g in range(GROUPS):
                    last = pe.transpose(bank[0][:, P * g:P * (g + 1)], y_t[:, g], ident)
                last.then_inc(yt_done, 1)

            def run(f, a):
                p = f.back(1)
                on = f.exists and f.first < tiles

                def expert(do, n):
                    if n >= 0 and on:
                        do(f, n)
                    if n < 0 and p.exists:
                        do(p, EXPERTS + n)

                def w2_slot(n):
                    if n % EXPERTS:
                        expert(w2_low, n - 1)
                    expert(w2_high, n)

                def warm(n):
                    if not f.exists:
                        keep_warm(n)

                expert(w1_product, -2)
                w2_slot(-4)
                if on:
                    route(f)
                expert(w1_product, -1)
                if a.exists:
                    transpose_xn1(a)
                warm(1)
                w2_slot(-3)
                if a.exists:
                    project_qk(a)
                    project_v(a)
                expert(w1_product, 0)
                if a.exists:
                    transpose_k(a)
                if on:
                    transpose_roots(f)
                if a.exists:
                    scores(a, 0, f)
                    scores(a, 1, f)
                w2_slot(-2)
                expert(w1_product, 1)
                if a.exists:
                    scores(a, 2, f)
                    scores(a, 3, f)
                w2_slot(-1)
                if a.exists:
                    state_updates(a)
                warm(7)
                expert(w2_low, -1)
                expert(w1_product, 2)
                transpose_y(p, a)
                w2_slot(0)
                if a.exists:
                    outputs(a, (0, 1))
                expert(w1_product, 3)
                if a.exists:
                    outputs(a, (2, 3))
                warm(1)
                w2_slot(1)
                if a.exists:
                    project_out(a, p)
                warm(9)
                expert(w1_product, 4)
                w2_slot(2)
                expert(w1_product, 5)
                w2_slot(3)
                if a.exists:
                    transpose_xn2(a)
                warm(3)

            pe.wait_ge(zeroed, 1)
            keep_warm(8)
            pe.wait_ge(first_loaded, 5 * DMA)
            steps(pe, run)

        @block.vector
        def _(dve):
            def norm_statistics(t, which, source):
                for g in range(GROUPS):
                    last = nc.vector.bn_stats(stats[:, which, g], source[:, g])
                last.then_inc(norm_step[which], 1)
                wait_apart(dve, norm_step[which], t.count(2, 1))
                for g in range(GROUPS):
                    last = nc.vector.bn_aggr(moments[:, which, g], stats[:, which, g])
                last.then_inc(norm_step[which], 1)
                dve.wait_ge(norm_step[which], t.count(2))
                nc.vector.tensor_scalar(variance[:, which], moments[:, which, :, 1], LN_EPS, None, ALU.add
                                        ).then_inc(variance_ready[which], 1)

            def normalise(t, which, source, target, ready):
                dve.wait_ge(rstd_ready[which], t.count(1))
                for g in range(GROUPS):
                    last = nc.vector.tensor_scalar(target[:, g], source[:, g], moments[:, which, g, 0:1],
                                                   rstd[:, which, g:g + 1], ALU.subtract, ALU.mult)
                last.then_inc(ready, 1)

            def statistics_x(a):
                dve.wait_ge(x_loaded[a.parity], a.count2(DMA))
                norm_statistics(a, 0, x_in[:, a.parity])

            def normalise_x(a):
                if a.back(1).exists:
                    dve.wait_ge(t1_done, a.back(1).count(1))
                normalise(a, 0, x_in[:, a.parity], xn1, xn1_ready)

            def scale_h(t, e):
                if e % (EXPERTS // PARTS) == 0:
                    dve.wait_ge(scale_loaded[t.parity][e // (EXPERTS // PARTS)], t.count2(DMA))
                dve.wait_ge(h_done, t.count(EXPERTS, e + 1))
                if EXPERTS * t.first + e >= 2:
                    dve.wait_ge(act_f_ready, t.count(EXPERTS, e - 1))
                nc.vector.scalar_tensor_tensor(
                    out=act_s[:, ring(t, e, 2)], in0=h_ps[:, ring(t, e, 2)], scalar=0.0,
                    in1=scale[:, t.parity, e].unsqueeze(1).to_broadcast([P, HALVES, TILE]),
                    op0=ALU.max, op1=ALU.mult).then_inc(act_s_ready, 1)

            def decay_q(a):
                if a.first == 0:
                    dve.wait_ge(first_loaded, 5 * DMA)
                dve.wait_ge(q_m_ready, a.count(1))
                if a.back(1).exists:
                    dve.wait_ge(av_done, a.back(1).count(1))
                nc.vector.tensor_tensor(
                    q_d[:].rearrange("p (c i) -> p c i", i=CHUNK), bank[1][:].rearrange("p (c i) -> p c i", i=CHUNK),
                    cst[:, C_DQ:C_DQ + CHUNK].unsqueeze(1).to_broadcast([P, CHUNKS, CHUNK]), ALU.mult
                ).then_inc(q_d_ready, 1)

            def low(t, e):
                n = slice(0 if e == DVE_ALONE else 1, HALVES)
                dve.wait_ge(act_f_ready, t.count(EXPERTS, e + 1))
                if EXPERTS * t.first + e >= 4:
                    dve.wait_ge(y_done, t.count(EXPERTS, e - 3))
                nc.vector.tensor_tensor(act_lo[:, ring(t, e, 4), n], act_f[:, ring(t, e, 2), n],
                                        act_hi[:, ring(t, e, 4), n].bitcast(F32), ALU.subtract
                                        ).then_inc(dve_low_ready, 1)

            def copy_v(a):
                dve.wait_ge(v_done, a.count(1))
                nc.vector.tensor_copy(v_z[:, :, ::3], bank[0][:].rearrange("p (n h d) -> p n h d", h=2, d=DH)
                                      ).then_inc(v_z_ready, 1)

            def decay_k(a):
                dve.wait_ge(kt_done, a.count(1))
                nc.vector.tensor_tensor(
                    k_d[:], bank[1][:].rearrange("p (g d) -> p g d", d=P),
                    cst[:, C_DK:C_DK + P].unsqueeze(1).to_broadcast([P, GROUPS, P]), ALU.mult
                ).then_inc(k_d_ready, 1)

            def decay_scores(a, pair):
                dve.wait_ge(qk_done, a.count(PAIRS, pair + 1))
                table = cst[:, C_DECAY + P * pair:C_DECAY + P * (pair + 1)]
                nc.vector.tensor_tensor(
                    attn[:, pair].rearrange("p g j i -> p g (j i)"),
                    score_bank[pair][:].rearrange("p (g n) -> p g n", n=P),
                    table.unsqueeze(1).to_broadcast([P, GROUPS, P]), ALU.mult).then_inc(attn_ready, 1)

            def scan_states(a):
                if a.back(1).exists:
                    dve.wait_ge(state_step, a.back(1).count(CHUNKS + 1))
                else:
                    dve.wait_ge(zeroed, 3)
                nc.vector.tensor_scalar(state[:, 0], state[:, CHUNKS], cst[:, bass.ds(a.index + C_LOW, 1)],
                                        cst[:, bass.ds(a.index + C_HIGH, 1)], ALU.max, ALU.min
                                        ).then_inc(state_step, 1)
                dve.wait_ge(u_done, a.count(1))
                for c in range(CHUNKS):
                    dve.wait_ge(state_step, a.count(CHUNKS + 1, c + 1))
                    nc.vector.scalar_tensor_tensor(
                        out=state[:, c + 1], in0=state[:, c], scalar=cst[:, C_DS:C_DS + 1],
                        in1=chunk_bank[c % 2][:, PW * (c // 2):PW * (c // 2 + 1)], op0=ALU.mult, op1=ALU.add
                    ).then_inc(state_step, 1)
                dve.wait_ge(state_step, a.count(CHUNKS + 1))
                nc.vector.tensor_tensor(
                    state_m[:], state[:, 0:CHUNKS],
                    cst[:, C_SMASK:C_SMASK + PW].unsqueeze(1).to_broadcast([P, CHUNKS, PW]), ALU.mult
                ).then_inc(state_ready, 1)

            def add_attention(a):
                dve.wait_ge(wo_done, a.count(1))
                nc.vector.tensor_tensor(x2[:, a.parity], bank[0][:].rearrange("p (g d) -> p g d", d=P),
                                        x_in[:, a.parity], ALU.add).then_inc(x2_ready, 1)
                dve.wait_ge(x2_ready, a.count(1))

            def low_x(a):
                dve.wait_ge(x_hi_ready, a.count(1))
                nc.vector.tensor_tensor(x_lo[:, a.parity], bank[1][:], x_hi[:, a.parity].bitcast(F32), ALU.subtract
                                        ).then_inc(x_lo_ready, 1)

            def shift_logits(a):
                dve.wait_ge(router_done, a.count(1))
                l_ps = bank[2][:, 0:GROUPS * EXPERTS].rearrange("p (g e) -> p g e", e=EXPERTS)
                nc.vector.tensor_reduce(top[:], l_ps, AX_X, ALU.max).then_inc(top_ready, 1)
                dve.wait_ge(top_ready, a.count(1))
                nc.vector.tensor_tensor(logits[:], l_ps, top[:].unsqueeze(2).to_broadcast([P, GROUPS, EXPERTS]),
                                        ALU.subtract).then_inc(logits_ready, 1)

            def by_expert(ap):
                return ap.unsqueeze(2).to_broadcast([P, GROUPS, EXPERTS])

            def choose(a):
                done = [0]

                def step(ins):
                    ins.then_inc(router_step, 1)
                    done[0] += 1

                def after(n):
                    dve.wait_ge(router_step, a.count(ROUTER_STEPS, n))

                iota = cst[:, C_IOTA:C_IOTA + EXPERTS].unsqueeze(1).to_broadcast([P, GROUPS, EXPERTS])
                dve.wait_ge(expd_ready, a.count(1))
                step(nc.vector.tensor_reduce(total[:], expd[:], AX_X, ALU.add))
                for g in range(GROUPS):
                    last = nc.vector.max(best[:, g], expd[:, g])
                step(last)
                after(2)
                step(nc.vector.scalar_tensor_tensor(out=denom[:, 0], in0=total[:], scalar=TOP_EPS,
                                                    in1=best[:, :, 0], op0=ALU.mult, op1=ALU.add))
                for g in range(GROUPS):
                    last = nc.vector.max_index(best_at[:, g], best[:, g], expd[:, g])
                step(last)
                after(3)
                step(nc.vector.tensor_tensor(denom[:, 1], denom[:, 0], best[:, :, 1], ALU.add))
                after(4)
                step(nc.vector.tensor_copy(best_f[:], best_at[:, :, 0:2]))
                after(5)
                step(nc.vector.reciprocal(r_denom[:], denom[:, 1]))
                after(6)
                for n in range(2):
                    last = nc.vector.tensor_tensor(chosen[:, n], iota, by_expert(best_f[:, :, n]), ALU.is_equal)
                step(last)
                after(7)
                nc.vector.tensor_tensor(share[:], best[:, :, 0:2], r_denom[:].unsqueeze(2).to_broadcast([P, GROUPS, 2]),
                                        ALU.mult).then_inc(share_ready, 1)
                assert done[0] == ROUTER_STEPS - 1

            def spread_roots(a):
                dve.wait_ge(root_ready, a.count(1))
                dve.wait_ge(router_step, a.count(ROUTER_STEPS, ROUTER_STEPS - 1))
                for n in range(2):
                    last = nc.vector.tensor_tensor(spread[:, n], chosen[:, n], by_expert(root[:, :, n]), ALU.mult)
                last.then_inc(router_step, 1)
                dve.wait_ge(router_step, a.count(ROUTER_STEPS))
                if a.back(1).exists:
                    dve.wait_ge(root_t_done, a.back(1).count(1))
                nc.vector.tensor_tensor(combine_r[:].rearrange("p e g -> p g e"), spread[:, 0], spread[:, 1],
                                        ALU.add).then_inc(combine_ready, 1)

            def add_experts(p):
                dve.wait_ge(yt_done, p.count(1))
                dve.wait_ge(out_free, p.count(DMA))
                nc.vector.tensor_tensor(out_sb[:], bank[0][:].rearrange("p (g d) -> p g d", d=P), x2[:, p.parity],
                                        ALU.add).then_inc(out_ready, 1)

            def run(f, a):
                p = f.back(1)
                on = f.exists and f.first < tiles

                def expert(do, n):
                    if n >= 0 and on:
                        do(f, n)
                    if n < 0 and p.exists:
                        do(p, EXPERTS + n)

                if a.exists and a.first != 1:
                    statistics_x(a)
                if on:
                    low_x(f)
                expert(scale_h, -3)
                if a.exists and a.first != 1:
                    normalise_x(a)
                expert(low, -4)
                if on:
                    shift_logits(f)
                    choose(f)
                expert(scale_h, -2)
                if a.exists:
                    decay_q(a)
                if on:
                    spread_roots(f)
                if a.exists:
                    copy_v(a)
                expert(low, -3)
                if a.exists:
                    decay_k(a)
                expert(scale_h, -1)
                if a.exists:
                    decay_scores(a, 0)
                    decay_scores(a, 1)
                expert(low, -2)
                if a.exists:
                    decay_scores(a, 2)
                expert(scale_h, 0)
                if a.exists:
                    decay_scores(a, 3)
                expert(low, -1)
                if a.exists:
                    scan_states(a)
                    if a.first == 0:
                        statistics_x(tile(1))
                        normalise_x(tile(1))
                expert(scale_h, 1)
                expert(low, 0)
                if p.exists:
                    add_experts(p)
                expert(scale_h, 2)
                expert(low, 1)
                expert(scale_h, 3)
                if a.exists:
                    add_attention(a)
                    norm_statistics(a, 1, x2[:, a.parity])
                expert(low, 2)
                if a.exists:
                    normalise(a, 1, x2[:, a.parity], xn2, xn2_ready)
                expert(scale_h, 4)
                expert(low, 3)

            nc.vector.memset(zeros[:], 0.0).then_inc(zeroed, 1)
            nc.vector.memset(v_z[:], 0.0).then_inc(zeroed, 1)
            nc.vector.memset(state[:, CHUNKS], 0.0).then_inc(zeroed, 1)
            dve.wait_ge(zeroed, 3)
            steps(dve, run)

        @block.scalar
        def _(act):
            act.wait_ge(zeroed, 1)
            nc.scalar.activation(table_load[:], zeros[:, 0:1], ACT.Exp)
            act.wait_ge(first_loaded, 5 * DMA)
            act.dma_start(wg_in[:], wg).then_inc(wg_loaded, DMA)
            act.dma_start(w1_in[:], w1.rearrange("e d h -> d e h")).then_inc(w1_loaded, DMA)
            act.dma_start(w2_in[:], w2.rearrange("e (n h) d -> h (e n) d", h=P)).then_inc(w2_loaded, DMA)

            def square(t, e):
                act.wait_ge(act_s_ready, t.count(EXPERTS, e + 1))
                if EXPERTS * t.first + e >= 4:
                    act.wait_ge(y_done, t.count(EXPERTS, e - 3))
                nc.scalar.activation(act_hi[:, ring(t, e, 4)], act_s[:, ring(t, e, 2)], ACT.Square
                                     ).then_inc(act_hi_ready, 1)
                if EXPERTS * t.first + e >= 2:
                    act.wait_ge(pool_low_ready, pool_lows(t, e - 1))
                    act.wait_ge(dve_low_ready, t.count(EXPERTS, e - 1))
                nc.scalar.activation(act_f[:, ring(t, e, 2)], act_s[:, ring(t, e, 2)], ACT.Square
                                     ).then_inc(act_f_ready, 1)

            def copy_xn1(a):
                act.wait_ge(t1_done, a.count(1))
                if a.back(1).exists:
                    act.wait_ge(v_done, a.back(1).count(1))
                nc.scalar.copy(xn1_t[:], bank[0][:]).then_inc(xn1_t_ready, 1)

            def mask_q(a):
                act.wait_ge(q_done, a.count(1))
                nc.scalar.activation(q_m[:, 0], bank[1][:], ACT.Copy, scale=cst[:, C_EVEN:C_EVEN + 1])
                nc.scalar.activation(q_m[:, 1], bank[1][:], ACT.Copy, scale=cst[:, C_ODD:C_ODD + 1]
                                     ).then_inc(q_m_ready, 1)

            def copy_k(a):
                act.wait_ge(k_done, a.count(1))
                nc.scalar.copy(k_t[:], bank[2][:]).then_inc(k_t_ready, 1)

            def copy_y(p):
                act.wait_ge(y_done, p.count(EXPERTS))
                if p.back(1).exists:
                    act.wait_ge(yt_done, p.back(1).count(1))
                nc.scalar.copy(y_t[:].rearrange("p g n -> p (g n)"), y_ps[:]).then_inc(y_t_ready, 1)

            def copy_o(a):
                act.wait_ge(av_done, a.count(1))
                for c in range(2):
                    last = nc.scalar.copy(o_t[:, :, c],
                                          chunk_bank[c][:, 0:TILE // 2].rearrange("p (g i) -> p g i", i=CHUNK))
                last.then_inc(o_t_ready, 1)

            def high_x(a):
                act.wait_ge(t2_done, a.count(1))
                if a.back(2).exists:
                    act.wait_ge(h_done, a.back(2).count(EXPERTS))
                nc.scalar.copy(x_hi[:, a.parity], bank[1][:]).then_inc(x_hi_ready, 1)

            def exponentiate(a):
                act.wait_ge(logits_ready, a.count(1))
                nc.scalar.activation(expd[:], logits[:], ACT.Exp).then_inc(expd_ready, 1)

            def high_weights(loaded, hi, whole):
                act.wait_ge(loaded, DMA)
                nc.scalar.copy(hi[:], whole[:]).then_inc(hi_split, 1)

            def copy_roots(a):
                act.wait_ge(root_t_done, a.count(1))
                if a.back(1).exists:
                    act.wait_ge(root_stored, a.back(1).count(DMA))
                nc.scalar.copy(combine_t[:], bank[2][0:EXPERTS * GROUPS, 0:P]).then_inc(root_t_ready, 1)

            def run(f, a):
                p = f.back(1)
                on = f.exists and f.first < tiles

                def expert(do, n):
                    if n >= 0 and on:
                        do(f, n)
                    if n < 0 and p.exists:
                        do(p, EXPERTS + n)

                expert(square, -3)
                if a.exists:
                    copy_xn1(a)
                if on:
                    exponentiate(f)
                if a.exists:
                    mask_q(a)
                    copy_k(a)
                expert(square, -2)
                if on:
                    copy_roots(f)
                if a.exists and a.first == 0:
                    high_weights(w1_loaded, w1_hi, w1_in)
                    high_weights(wg_loaded, wg_hi, wg_in)
                    high_weights(w2_loaded, w2_hi, w2_in)
                expert(square, -1)
                expert(square, 0)
                if p.exists:
                    copy_y(p)
                expert(square, 1)
                if a.exists:
                    copy_o(a)
                expert(square, 2)
                expert(square, 3)
                if a.exists:
                    high_x(a)
                expert(square, 4)

            act.wait_ge(first_loaded, 5 * DMA)
            steps(act, run)

        @block.gpsimd
        def _(pool):
            def low(t, e):
                if e == DVE_ALONE:
                    return
                pool.wait_ge(act_f_ready, t.count(EXPERTS, e + 1))
                if EXPERTS * t.first + e >= 4:
                    pool.wait_ge(y_done, t.count(EXPERTS, e - 3))
                nc.gpsimd.tensor_tensor(act_lo[:, ring(t, e, 4), 0], act_f[:, ring(t, e, 2), 0],
                                        act_hi[:, ring(t, e, 4), 0].bitcast(F32), ALU.subtract
                                        ).then_inc(pool_low_ready, 1)

            def root_variance(t, which):
                pool.wait_ge(variance_ready[which], t.count(1))
                nc.gpsimd.tensor_tensor(rstd[:, which], variance[:, which], minus_half[:], ALU.pow
                                        ).then_inc(rstd_ready[which], 1)

            def root_shares(t):
                pool.wait_ge(share_ready, t.count(1))
                nc.gpsimd.tensor_tensor(root[:].rearrange("p g n -> p (g n)"), share[:].rearrange("p g n -> p (g n)"),
                                        half[:], ALU.pow).then_inc(root_ready, 1)

            def split(hi, lo, whole, n):
                pool.wait_ge(hi_split, n)
                nc.gpsimd.tensor_tensor(lo[:], whole[:], hi[:].bitcast(F32), ALU.subtract).then_inc(lo_split, 1)

            def run(f, a):
                p = f.back(1)
                on = f.exists and f.first < tiles

                def expert(do, n):
                    if n >= 0 and on:
                        do(f, n)
                    if n < 0 and p.exists:
                        do(p, EXPERTS + n)

                if a.exists and a.first != 1:
                    root_variance(a, 0)
                expert(low, -4)
                expert(low, -3)
                if on:
                    root_shares(f)
                if a.exists and a.first == 0:
                    split(w1_hi, w1_lo, w1_in, 1)
                    split(wg_hi, wg_lo, wg_in, 2)
                    split(w2_hi, w2_lo, w2_in, 3)
                    root_variance(tile(1), 0)
                for e in range(-2, 2):
                    expert(low, e)
                if a.exists:
                    root_variance(a, 1)
                expert(low, 3)

            nc.gpsimd.memset(minus_half[:], -0.5)
            nc.gpsimd.memset(half[:], 0.5).then_inc(exponents_set, 1)
            pool.wait_ge(exponents_set, 1)
            steps(pool, run)


def constant_table():
    import numpy as np

    gamma = 1.0 - np.exp2(-5.0 - np.arange(HEADS))
    i = np.arange(CHUNK)
    t = np.zeros((P, C_ALL), np.float64)
    t[:, C_IDENT:C_IDENT + P] = np.eye(P)
    diff = i[None, :] - i[:, None]
    decay = np.where(diff >= 0, gamma[:, None, None] ** np.maximum(diff, 0), 0.0) * DH ** -0.5
    t[:, C_DECAY:C_DECAY + HEADS * CHUNK] = np.tile(decay.transpose(1, 0, 2).reshape(CHUNK, -1), (2, 1))
    head = np.arange(P) // DH
    t[:, C_DQ:C_DQ + CHUNK] = gamma[head][:, None] ** (i[None, :] + 1) * DH ** -0.5
    t[:, C_DK:C_DK + P] = np.tile(gamma[head][None, :] ** (CHUNK - 1 - i[:, None]), (2, 1))
    t[:, C_EVEN] = head % 2 == 0
    t[:, C_ODD] = head % 2 == 1
    t[:, C_DS] = gamma[head] ** CHUNK
    t[:, C_SMASK:C_SMASK + PW] = (head % 2)[:, None] == (np.arange(PW) // DH)[None, :]
    fresh = np.arange(8) % 4 == 0
    t[:, C_LOW:C_LOW + 8] = np.where(fresh, 0.0, -BIG)
    t[:, C_HIGH:C_HIGH + 8] = np.where(fresh, 0.0, BIG)
    t[:, C_IOTA:C_IOTA + EXPERTS] = np.arange(EXPERTS)
    return t.astype(np.float32)


def kernel(**inputs):
    import numpy as np
    import concourse.bacc as bacc
    from concourse.bass_utils import run_bass_kernel_spmd

    nc = bacc.Bacc("TRN2", target_bir_lowering=False, num_devices=1)
    names = {"x": "L0_attn_hidden_states", "wq": "L0_attn_Wq", "wk": "L0_attn_Wk", "wv": "L0_attn_Wv",
             "wo": "L0_attn_Wo", "wg": "L0_ffn_Wg", "w1": "L0_ffn_W1", "w2": "L0_ffn_W2"}
    arrays = {k: np.ascontiguousarray(inputs[n]) for k, n in names.items()}
    arrays["constants"] = constant_table()
    args = {k: nc.dram_tensor(k, a.shape, F32, kind="ExternalInput").ap() for k, a in arrays.items()}
    scratch = nc.dram_tensor("scratch", (2, EXPERTS * TILE), F32, kind="Internal").ap()
    out = nc.dram_tensor("out", arrays["x"].shape, F32, kind="ExternalOutput").ap()
    build(nc, scratch=scratch, out=out, **args)
    result = run_bass_kernel_spmd(nc, [arrays], core_ids=[0])
    return result.results[0]["out"]
```
